# Optimizing a Trainium2 kernel written in Bass

```python
import numpy as np
import jax
import jax.numpy as jnp

def _softmax(x, axis=-1):
    return jax.nn.softmax(x, axis=axis)

def _gelu(x):
    return jax.nn.gelu(x, approximate=True)

def _silu(x):
    return jax.nn.silu(x)

def _sigmoid(x):
    return jax.nn.sigmoid(x)

def _layernorm(x, axis=-1, eps=1e-05):
    m = jnp.mean(x, axis=axis, keepdims=True)
    v = jnp.var(x, axis=axis, keepdims=True)
    return (x - m) / jnp.sqrt(v + eps)

def _scatter_add(tgt, idx, src, axis=0):
    return tgt.at[idx].add(src)

def _segment_sum(src, seg, n):
    return jax.ops.segment_sum(src, seg, n)
kernel_name = 'mk_rec_standalone_d1_rec_r8_d40e78'

def setup_inputs(seed: int=0):
    np.random.seed(seed)
    _w = jnp.asarray

    def _rec_inputs():
        import jax
        import jax.numpy as jnp
        _rk = jax.random.key(seed)
        r_inputs = -0.000612844 + 1.00049 * jax.random.normal(jax.random.fold_in(_rk, 1), (512, 50, 32), jnp.float32)
        return r_inputs
    r_inputs = _rec_inputs()

    def _L0_rec_setup():
        import jax, jax.numpy as jnp
        import numpy as np
        key = jax.random.key(seed)
        k1, k2 = jax.random.split(key)
        B, F, E = (256, 50, 32)
        inputs = jax.random.normal(k1, (B, F, E), dtype=jnp.float32)
        limit = np.sqrt(6.0 / (E + E)).astype(np.float32)
        bilinear_kernel = jax.random.uniform(k2, (F, E, E), dtype=jnp.float32, minval=-limit, maxval=limit)
        return {'inputs': inputs, 'bilinear_kernel': bilinear_kernel, 'field_size': F, 'embedding_size': E}
    _L0_rec_all = _L0_rec_setup()
    _L0_rec_in = {k: v for k, v in _L0_rec_all.items() if k in ('bilinear_kernel',)}
    del _L0_rec_all
    return {'r_inputs': r_inputs, 'L0_rec_bilinear_kernel': _L0_rec_in['bilinear_kernel']}

def reference(r_inputs, L0_rec_bilinear_kernel):
    import jax
    import jax.numpy as jnp

    def _L0_rec_ref(inputs, bilinear_kernel, field_size, embedding_size):
        import jax, jax.numpy as jnp
        import numpy as np
        x = jnp.reshape(inputs, (-1, field_size, embedding_size))
        proj = jnp.einsum('bfe,feg->bfg', x, bilinear_kernel)
        out = proj[:, :, None, :] * x[:, None, :, :]
        B = x.shape[0]
        return out.reshape(B, field_size * field_size, embedding_size)
    y = _L0_rec_ref(r_inputs, L0_rec_bilinear_kernel, 50, 32)
    return y

_drawn_inputs = setup_inputs


def setup_inputs(seed=0):
    import zlib

    import numpy as np

    out = dict(_drawn_inputs(seed))
    spreads = {}
    factors = {}
    for name, (base, spread) in spreads.items():
        noise = np.random.default_rng([zlib.crc32(name.encode()), seed]).standard_normal(out[name].shape)
        drawn = base * np.exp(spread * noise) if base else spread * noise
        out[name] = jnp.asarray(drawn.astype(out[name].dtype))
    for name, factor in factors.items():
        out[name] = (out[name] * factor).astype(out[name].dtype)
    return out
```

```python
import concourse.bass as bass
from concourse import mybir
from contextlib import ExitStack

P = 128


def field_products_kernel(nc: bass.Bass, x: bass.AP, w: bass.AP, out: bass.AP):
    fp32 = mybir.dt.float32
    ALU = mybir.AluOpType

    B, F, E = x.shape
    TILES = B // P
    ROW = F * E
    PAIRS = F // 2
    K = 2 * E
    RING = 5
    BLOCKS = PAIRS // RING
    BCOLS = RING * K
    PIECE = 2 * ROW
    assert TILES * P == B and PAIRS * 2 == F and BLOCKS * RING == PAIRS

    x_rows = x.rearrange("(t p) f e -> p t (f e)", p=P)
    w_rows = w.rearrange("f e g -> e f g")
    out_rows = out.rearrange("(t p) (c q) e -> t p c (q e)", p=P, c=PAIRS)

    with ExitStack() as ctx:
        def sb(name, shape):
            return ctx.enter_context(nc.sbuf_tensor(name, shape, fp32))

        def ps(name, shape):
            return ctx.enter_context(nc.psum_tensor(name, shape, fp32))

        def sem(name):
            return ctx.enter_context(nc.semaphore(name))

        x_sb = sb("x_sb", [P, TILES * ROW])
        proj_sb = sb("proj_sb", [P, TILES * ROW])
        w_sb = sb("w_sb", [E, ROW])
        ident = sb("ident", [P, P])
        x_block = sb("x_block", [P, BCOLS])
        xT = sb("xT", [E, 2 * RING * P])
        ring = [sb(f"ring{s}", [P, PIECE]) for s in range(RING)]

        xT_ps = ps("xT_ps", [E, 3 * 512])
        proj_ps = ps("proj_ps", [P, 512])

        x0_loaded = sem("x0_loaded")
        x_loaded = sem("x_loaded")
        w_loaded = sem("w_loaded")
        ident_zero = sem("ident_zero")
        ident_ready = sem("ident_ready")
        block_copied = sem("block_copied")
        transposed = sem("transposed")
        xT_ready = sem("xT_ready")
        projected = sem("projected")
        proj_ready = sem("proj_ready")
        filled = sem("filled")
        stored = [sem(f"stored{s}") for s in range(RING)]

        FIRST_LOTS = [(0, 1), (1, RING)]

        def tiles_and_blocks(eng, first, block):
            first()
            with eng.Fori(1, BLOCKS) as k:
                block(0, k, k)
            with eng.Fori(1, TILES) as t:
                with eng.Fori(0, BLOCKS) as k:
                    block(t, k, t * BLOCKS + k)

        with nc.Block() as block:

            @block.sync
            def _(sp):
                sp.dma_start(x_sb[:, 0:ROW], x_rows[:, 0, :]).then_inc(x0_loaded, 16)
                sp.dma_start(x_sb[:, ROW:TILES * ROW].rearrange("p (t c) -> p t c", c=ROW),
                             x_rows[:, 1:TILES, :]).then_inc(x_loaded, 16)

                def store(t, k, u):
                    for s in range(RING):
                        sp.wait_ge(filled, u * RING + s + 1)
                        sp.dma_start(out_rows[bass.ds(t, 1), :, bass.ds(k * RING + s, 1), :],
                                     ring[s][:, :]).then_inc(stored[s], 16)

                tiles_and_blocks(sp, lambda: store(0, 0, 0), store)
                for s in range(RING):
                    sp.wait_ge(stored[s], 16 * TILES * BLOCKS)

            @block.gpsimd
            def _(pool):
                nc.gpsimd.memset(ident[:, :], 0.0).then_inc(ident_zero, 1)
                pool.wait_ge(ident_zero, 1)
                nc.gpsimd.affine_select(out=ident[:, :], in_=ident[:, :], compare_op=ALU.not_equal, fill=1.0,
                                        base=0, pattern=[[-1, P]], channel_multiplier=1).then_inc(ident_ready, 1)

            @block.vector
            def _(dve):
                def multiply(x_col, proj_col, s):
                    x_in = x_sb[:, bass.ds(x_col, ROW)].rearrange("p (a c) -> p a c", a=1)
                    proj_in = proj_sb[:, bass.ds(proj_col, K)].rearrange("p (i a g) -> p i a g", i=2, a=1)
                    nc.vector.tensor_tensor(
                        out=ring[s][:, :].rearrange("p (i j e) -> p i j e", i=2, e=E),
                        in0=x_in.rearrange("p a (j e) -> p a j e", e=E).to_broadcast([P, 2, F, E]),
                        in1=proj_in.to_broadcast([P, 2, F, E]),
                        op=ALU.mult).then_inc(filled, 1)

                def first():
                    dve.wait_ge(x0_loaded, 16)
                    for lot, (a, b) in enumerate(FIRST_LOTS):
                        dve.wait_ge(proj_ready, lot + 1)
                        for s in range(a, b):
                            multiply(0, s * K, s)

                def products(t, k, u):
                    dve.wait_ge(proj_ready, u + 2)
                    for s in range(RING):
                        dve.wait_ge(stored[s], u * 16)
                        multiply(t * ROW, u * BCOLS + s * K, s)

                first()
                with dve.Fori(1, BLOCKS) as k:
                    products(0, k, k)
                dve.wait_ge(x_loaded, 16)
                with dve.Fori(1, TILES) as t:
                    with dve.Fori(0, BLOCKS) as k:
                        products(t, k, t * BLOCKS + k)

            @block.scalar
            def _(act):
                act.dma_start(w_sb[:, :].rearrange("e (f g) -> e f g", g=E), w_rows).then_inc(w_loaded, 16)

                def evacuate(lot, a, b, col):
                    act.wait_ge(transposed, lot + 1)
                    nc.scalar.copy(xT[:, 2 * a * P:2 * b * P],
                                   xT_ps[:, 2 * a * P:2 * b * P]).then_inc(xT_ready, 1)
                    act.wait_ge(projected, lot + 1)
                    nc.scalar.copy(proj_sb[:, bass.ds(col, (b - a) * K)],
                                   proj_ps[:, a * K:b * K]).then_inc(proj_ready, 1)

                def first():
                    for lot, (a, b) in enumerate(FIRST_LOTS):
                        evacuate(lot, a, b, a * K)

                def project(t, k, u):
                    nc.scalar.copy(x_block[:, :], x_sb[:, bass.ds(u * BCOLS, BCOLS)]).then_inc(block_copied, 1)
                    evacuate(u + 1, 0, RING, u * BCOLS)

                first()
                with act.Fori(1, BLOCKS) as k:
                    project(0, k, k)
                act.wait_ge(x_loaded, 16)
                with act.Fori(1, TILES) as t:
                    with act.Fori(0, BLOCKS) as k:
                        project(t, k, t * BLOCKS + k)

            @block.tensor
            def _(pe):
                def project(lot, a, b, src, w_col):
                    for f in range(2 * a, 2 * b):
                        last = nc.tensor.transpose(xT_ps[:, f * P:(f + 1) * P], src[:, f * E:(f + 1) * E],
                                                   ident[:, :])
                    last.then_inc(transposed, 1)
                    pe.wait_ge(xT_ready, lot + 1)
                    if not isinstance(lot, int) or lot > 0:
                        pe.wait_ge(proj_ready, lot)
                    for f in range(2 * a, 2 * b):
                        last = nc.tensor.matmul(proj_ps[:, f * E:(f + 1) * E], xT[:, f * P:(f + 1) * P],
                                                w_sb[:, bass.ds(w_col + (f - 2 * a) * E, E)],
                                                start=True, stop=True)
                    last.then_inc(projected, 1)

                pe.wait_ge(ident_ready, 1)
                pe.wait_ge(x0_loaded, 16)
                pe.wait_ge(w_loaded, 16)
                for lot, (a, b) in enumerate(FIRST_LOTS):
                    project(lot, a, b, x_sb, a * K)

                def block_step(t, k, u):
                    pe.wait_ge(block_copied, u)
                    project(u + 1, 0, RING, x_block, k * BCOLS)

                tiles_and_blocks(pe, lambda: None, block_step)


_INS = ['r_inputs', 'L0_rec_bilinear_kernel']


def kernel(**inputs):
    import numpy as _np
    import concourse.bacc as _bacc
    from concourse import mybir as _mybir
    from concourse.bass_utils import run_bass_kernel_spmd as _run

    nc = _bacc.Bacc("TRN2", target_bir_lowering=False, num_devices=1)
    arrays, args = {}, []
    for name in _INS:
        a = _np.ascontiguousarray(inputs[name])
        arrays[f"in_{name}_dram"] = a
        args.append(nc.dram_tensor(f"in_{name}_dram", a.shape, _mybir.dt.from_np(a.dtype), kind="ExternalInput").ap())
    b, f, e = inputs['r_inputs'].shape
    out = nc.dram_tensor("out_0_dram", (b, f * f, e), _mybir.dt.float32, kind="ExternalOutput").ap()
    field_products_kernel(nc, *args, out)
    r = _run(nc, [arrays], core_ids=[0])
    return r.results[0]["out_0_dram"]
```

```python
import concourse.bass as bass
from concourse import mybir
from contextlib import ExitStack

P = 128


def field_products_kernel(nc: bass.Bass, x: bass.AP, w: bass.AP, out: bass.AP):
    fp32 = mybir.dt.float32
    ALU = mybir.AluOpType

    B, F, E = x.shape
    TILES = B // P
    ROW = F * E
    PAIRS = F // 2
    K = 2 * E
    RING = 5
    BLOCKS = PAIRS // RING
    BCOLS = RING * K
    PIECE = 2 * ROW
    assert TILES * P == B and PAIRS * 2 == F and BLOCKS * RING == PAIRS

    x_rows = x.rearrange("(t p) f e -> p t (f e)", p=P)
    w_rows = w.rearrange("f e g -> e f g")
    out_rows = out.rearrange("(t p) (c q) e -> t p c (q e)", p=P, c=PAIRS)

    with ExitStack() as ctx:
        def sb(name, shape):
            return ctx.enter_context(nc.sbuf_tensor(name, shape, fp32))

        def ps(name, shape):
            return ctx.enter_context(nc.psum_tensor(name, shape, fp32))

        def sem(name):
            return ctx.enter_context(nc.semaphore(name))

        x_sb = sb("x_sb", [P, TILES * ROW])
        proj_sb = sb("proj_sb", [P, TILES * ROW])
        w_sb = sb("w_sb", [E, ROW])
        ident = sb("ident", [P, P])
        x_block = sb("x_block", [P, BCOLS])
        xT = sb("xT", [E, 2 * RING * P])
        ring = [sb(f"ring{s}", [P, PIECE]) for s in range(RING)]

        xT_ps = ps("xT_ps", [E, 3 * 512])
        proj_ps = ps("proj_ps", [P, 512])

        x_head_loaded = sem("x_head_loaded")
        x_tile_loaded = sem("x_tile_loaded")
        x_loaded = sem("x_loaded")
        w_head_loaded = sem("w_head_loaded")
        w_loaded = sem("w_loaded")
        ident_zero = sem("ident_zero")
        ident_ready = sem("ident_ready")
        block_copied = sem("block_copied")
        transposed = sem("transposed")
        xT_ready = sem("xT_ready")
        projected = sem("projected")
        proj_ready = sem("proj_ready")
        filled = sem("filled")
        half_filled = sem("half_filled")
        half_stored = sem("half_stored")
        stored = [sem(f"stored{s}") for s in range(RING)]

        FIRST_LOTS = [(0, 1), (1, RING)]
        FIRST_AT = [0, 512]

        def tiles_and_blocks(eng, first, block):
            first()
            with eng.Fori(1, BLOCKS) as k:
                block(0, k, k)
            with eng.Fori(1, TILES) as t:
                with eng.Fori(0, BLOCKS) as k:
                    block(t, k, t * BLOCKS + k)

        with nc.Block() as block:

            @block.sync
            def _(sp):
                sp.dma_start(x_sb[:, 0:BCOLS], x_rows[:, 0, 0:BCOLS]).then_inc(x_head_loaded, 16)
                sp.dma_start(x_sb[:, BCOLS:ROW], x_rows[:, 0, BCOLS:ROW]).then_inc(x_tile_loaded, 16)
                sp.dma_start(x_sb[:, ROW:TILES * ROW].rearrange("p (t c) -> p t c", c=ROW),
                             x_rows[:, 1:TILES, :]).then_inc(x_loaded, 16)

                def store(t, k, u):
                    for s in range(RING):
                        sp.wait_ge(filled, u * RING + s + 1)
                        sp.dma_start(out_rows[bass.ds(t, 1), :, bass.ds(k * RING + s, 1), :],
                                     ring[s][:, :]).then_inc(stored[s], 16)

                def first():
                    half = PIECE // 2
                    sp.wait_ge(half_filled, 1)
                    sp.dma_start(out_rows[0, :, 0, 0:half], ring[0][:, 0:half]).then_inc(half_stored, 16)
                    sp.wait_ge(filled, 1)
                    sp.dma_start(out_rows[0, :, 0, half:PIECE], ring[0][:, half:PIECE]).then_inc(stored[0], 16)
                    for s in range(1, RING):
                        sp.wait_ge(filled, s + 1)
                        sp.dma_start(out_rows[0, :, s, :], ring[s][:, :]).then_inc(stored[s], 16)

                tiles_and_blocks(sp, first, store)
                sp.wait_ge(half_stored, 16)
                for s in range(RING):
                    sp.wait_ge(stored[s], 16 * TILES * BLOCKS)

            @block.gpsimd
            def _(pool):
                nc.gpsimd.memset(ident[:, :], 0.0).then_inc(ident_zero, 1)
                pool.wait_ge(ident_zero, 1)
                nc.gpsimd.affine_select(out=ident[:, :], in_=ident[:, :], compare_op=ALU.not_equal, fill=1.0,
                                        base=0, pattern=[[-1, P]], channel_multiplier=1).then_inc(ident_ready, 1)

            @block.vector
            def _(dve):
                def multiply(x_col, proj_col, buffer, fields):
                    return nc.vector.tensor_tensor(
                        out=buffer.rearrange("p (i j e) -> p i j e", i=fields, e=E),
                        in0=x_sb[:, bass.ds(x_col, ROW)].rearrange("p (a j e) -> p a j e", a=1, e=E)
                        .to_broadcast([P, fields, F, E]),
                        in1=proj_sb[:, bass.ds(proj_col, fields * E)].rearrange("p (i a g) -> p i a g", a=1, g=E)
                        .to_broadcast([P, fields, F, E]),
                        op=ALU.mult)

                def first():
                    half = PIECE // 2
                    dve.wait_ge(x_head_loaded, 16)
                    dve.wait_ge(x_tile_loaded, 16)
                    dve.wait_ge(proj_ready, 1)
                    multiply(0, 0, ring[0][:, 0:half], 1).then_inc(half_filled, 1)
                    multiply(0, E, ring[0][:, half:PIECE], 1).then_inc(filled, 1)
                    dve.wait_ge(proj_ready, 2)
                    for s in range(1, RING):
                        multiply(0, s * K, ring[s][:, :], 2).then_inc(filled, 1)
                    dve.wait_ge(half_stored, 16)

                def products(t, k, u):
                    dve.wait_ge(proj_ready, u + 2)
                    for s in range(RING):
                        dve.wait_ge(stored[s], u * 16)
                        multiply(t * ROW, u * BCOLS + s * K, ring[s][:, :], 2).then_inc(filled, 1)

                first()
                with dve.Fori(1, BLOCKS) as k:
                    products(0, k, k)
                dve.wait_ge(x_loaded, 16)
                with dve.Fori(1, TILES) as t:
                    with dve.Fori(0, BLOCKS) as k:
                        products(t, k, t * BLOCKS + k)

            @block.scalar
            def _(act):
                w_fields = w_sb[:, :].rearrange("e (f g) -> e f g", g=E)
                act.dma_start(w_fields[:, 0:2 * RING, :], w_rows[:, 0:2 * RING, :]).then_inc(w_head_loaded, 16)
                act.dma_start(w_fields[:, 2 * RING:F, :], w_rows[:, 2 * RING:F, :]).then_inc(w_loaded, 16)

                def evacuate(lot, a, b, col, at=0):
                    act.wait_ge(transposed, lot + 1)
                    nc.scalar.copy(xT[:, 2 * a * P:2 * b * P],
                                   xT_ps[:, at:at + 2 * (b - a) * P]).then_inc(xT_ready, 1)
                    act.wait_ge(projected, lot + 1)
                    nc.scalar.copy(proj_sb[:, bass.ds(col, (b - a) * K)],
                                   proj_ps[:, a * K:b * K]).then_inc(proj_ready, 1)

                def first():
                    for lot, (a, b) in enumerate(FIRST_LOTS):
                        evacuate(lot, a, b, a * K, FIRST_AT[lot])

                def project(t, k, u):
                    nc.scalar.copy(x_block[:, :], x_sb[:, bass.ds(u * BCOLS, BCOLS)]).then_inc(block_copied, 1)
                    evacuate(u + 1, 0, RING, u * BCOLS)

                first()
                act.wait_ge(x_tile_loaded, 16)
                with act.Fori(1, BLOCKS) as k:
                    project(0, k, k)
                act.wait_ge(x_loaded, 16)
                with act.Fori(1, TILES) as t:
                    with act.Fori(0, BLOCKS) as k:
                        project(t, k, t * BLOCKS + k)

            @block.tensor
            def _(pe):
                def transpose(a, b, src, at=0):
                    for i, f in enumerate(range(2 * a, 2 * b)):
                        last = nc.tensor.transpose(xT_ps[:, at + i * P:at + (i + 1) * P],
                                                   src[:, f * E:(f + 1) * E], ident[:, :])
                    last.then_inc(transposed, 1)

                def project(lot, a, b, w_col):
                    pe.wait_ge(xT_ready, lot + 1)
                    if not isinstance(lot, int) or lot > 0:
                        pe.wait_ge(proj_ready, lot)
                    for f in range(2 * a, 2 * b):
                        last = nc.tensor.matmul(proj_ps[:, f * E:(f + 1) * E], xT[:, f * P:(f + 1) * P],
                                                w_sb[:, bass.ds(w_col + (f - 2 * a) * E, E)],
                                                start=True, stop=True)
                    last.then_inc(projected, 1)

                pe.wait_ge(ident_ready, 1)
                pe.wait_ge(x_head_loaded, 16)
                for lot, (a, b) in enumerate(FIRST_LOTS):
                    transpose(a, b, x_sb, FIRST_AT[lot])
                pe.wait_ge(w_head_loaded, 16)
                for lot, (a, b) in enumerate(FIRST_LOTS):
                    project(lot, a, b, a * K)
                pe.wait_ge(w_loaded, 16)

                def block_step(t, k, u):
                    pe.wait_ge(block_copied, u)
                    transpose(0, RING, x_block)
                    project(u + 1, 0, RING, k * BCOLS)

                tiles_and_blocks(pe, lambda: None, block_step)


_INS = ['r_inputs', 'L0_rec_bilinear_kernel']


def kernel(**inputs):
    import numpy as _np
    import concourse.bacc as _bacc
    from concourse import mybir as _mybir
    from concourse.bass_utils import run_bass_kernel_spmd as _run

    nc = _bacc.Bacc("TRN2", target_bir_lowering=False, num_devices=1)
    arrays, args = {}, []
    for name in _INS:
        a = _np.ascontiguousarray(inputs[name])
        arrays[f"in_{name}_dram"] = a
        args.append(nc.dram_tensor(f"in_{name}_dram", a.shape, _mybir.dt.from_np(a.dtype), kind="ExternalInput").ap())
    b, f, e = inputs['r_inputs'].shape
    out = nc.dram_tensor("out_0_dram", (b, f * f, e), _mybir.dt.float32, kind="ExternalOutput").ap()
    field_products_kernel(nc, *args, out)
    r = _run(nc, [arrays], core_ids=[0])
    return r.results[0]["out_0_dram"]
```
